# Optimizing a Trainium2 kernel written in Bass

```python
import numpy as np
import jax
import jax.numpy as jnp

def _softmax(x, axis=-1):
    return jax.nn.softmax(x, axis=axis)

def _gelu(x):
    return jax.nn.gelu(x, approximate=True)

def _silu(x):
    return jax.nn.silu(x)

def _sigmoid(x):
    return jax.nn.sigmoid(x)

def _layernorm(x, axis=-1, eps=1e-05):
    m = jnp.mean(x, axis=axis, keepdims=True)
    v = jnp.var(x, axis=axis, keepdims=True)
    return (x - m) / jnp.sqrt(v + eps)

def _scatter_add(tgt, idx, src, axis=0):
    return tgt.at[idx].add(src)

def _segment_sum(src, seg, n):
    return jax.ops.segment_sum(src, seg, n)
kernel_name = 'mk_dlrm_tower_d1_rec_r8_f29b60'

def setup_inputs(seed: int=0):
    np.random.seed(seed)
    _w = jnp.asarray

    def _rec_inputs():
        import jax
        import jax.numpy as jnp
        _tk = jax.random.key(seed)
        ids = jnp.stack([jax.random.randint(jax.random.fold_in(_tk, 200 + f), (2048,), 0, v, jnp.int32) for f, v in enumerate([1000, 125000, 12500, 1250, 12500, 1000, 1250, 1000, 1000, 1000, 12500, 1000, 1250, 1250, 1250, 1000, 1000, 12500, 1250, 1250, 1000, 1000, 1250, 1000, 1250, 12500])], axis=1)
        tbl_0 = 0.05 * jax.random.normal(jax.random.fold_in(_tk, 500 + 0), (1000, 128), jnp.float32)
        tbl_1 = 0.05 * jax.random.normal(jax.random.fold_in(_tk, 500 + 1), (125000, 128), jnp.float32)
        tbl_2 = 0.05 * jax.random.normal(jax.random.fold_in(_tk, 500 + 2), (12500, 128), jnp.float32)
        tbl_3 = 0.05 * jax.random.normal(jax.random.fold_in(_tk, 500 + 3), (1250, 128), jnp.float32)
        tbl_4 = 0.05 * jax.random.normal(jax.random.fold_in(_tk, 500 + 4), (12500, 128), jnp.float32)
        tbl_5 = 0.05 * jax.random.normal(jax.random.fold_in(_tk, 500 + 5), (1000, 128), jnp.float32)
        tbl_6 = 0.05 * jax.random.normal(jax.random.fold_in(_tk, 500 + 6), (1250, 128), jnp.float32)
        tbl_7 = 0.05 * jax.random.normal(jax.random.fold_in(_tk, 500 + 7), (1000, 128), jnp.float32)
        tbl_8 = 0.05 * jax.random.normal(jax.random.fold_in(_tk, 500 + 8), (1000, 128), jnp.float32)
        tbl_9 = 0.05 * jax.random.normal(jax.random.fold_in(_tk, 500 + 9), (1000, 128), jnp.float32)
        tbl_10 = 0.05 * jax.random.normal(jax.random.fold_in(_tk, 500 + 10), (12500, 128), jnp.float32)
        tbl_11 = 0.05 * jax.random.normal(jax.random.fold_in(_tk, 500 + 11), (1000, 128), jnp.float32)
        tbl_12 = 0.05 * jax.random.normal(jax.random.fold_in(_tk, 500 + 12), (1250, 128), jnp.float32)
        tbl_13 = 0.05 * jax.random.normal(jax.random.fold_in(_tk, 500 + 13), (1250, 128), jnp.float32)
        tbl_14 = 0.05 * jax.random.normal(jax.random.fold_in(_tk, 500 + 14), (1250, 128), jnp.float32)
        tbl_15 = 0.05 * jax.random.normal(jax.random.fold_in(_tk, 500 + 15), (1000, 128), jnp.float32)
        tbl_16 = 0.05 * jax.random.normal(jax.random.fold_in(_tk, 500 + 16), (1000, 128), jnp.float32)
        tbl_17 = 0.05 * jax.random.normal(jax.random.fold_in(_tk, 500 + 17), (12500, 128), jnp.float32)
        tbl_18 = 0.05 * jax.random.normal(jax.random.fold_in(_tk, 500 + 18), (1250, 128), jnp.float32)
        tbl_19 = 0.05 * jax.random.normal(jax.random.fold_in(_tk, 500 + 19), (1250, 128), jnp.float32)
        tbl_20 = 0.05 * jax.random.normal(jax.random.fold_in(_tk, 500 + 20), (1000, 128), jnp.float32)
        tbl_21 = 0.05 * jax.random.normal(jax.random.fold_in(_tk, 500 + 21), (1000, 128), jnp.float32)
        tbl_22 = 0.05 * jax.random.normal(jax.random.fold_in(_tk, 500 + 22), (1250, 128), jnp.float32)
        tbl_23 = 0.05 * jax.random.normal(jax.random.fold_in(_tk, 500 + 23), (1000, 128), jnp.float32)
        tbl_24 = 0.05 * jax.random.normal(jax.random.fold_in(_tk, 500 + 24), (1250, 128), jnp.float32)
        tbl_25 = 0.05 * jax.random.normal(jax.random.fold_in(_tk, 500 + 25), (12500, 128), jnp.float32)
        _rk = jax.random.fold_in(_tk, 7)
        r_dense_features = -0.000520686 + 1.00062 * jax.random.normal(jax.random.fold_in(_rk, 101), (2048, 128), jnp.float32)
        W_top1 = 0.0405887 * jax.random.normal(jax.random.fold_in(_tk, 801), (607, 512), jnp.float32)
        W_top2 = 0.0441942 * jax.random.normal(jax.random.fold_in(_tk, 802), (512, 256), jnp.float32)
        W_top3 = 0.0625 * jax.random.normal(jax.random.fold_in(_tk, 803), (256, 1), jnp.float32)
        b_top1 = jnp.zeros((512,), jnp.float32)
        b_top2 = jnp.zeros((256,), jnp.float32)
        return (r_dense_features, ids, tbl_0, tbl_1, tbl_2, tbl_3, tbl_4, tbl_5, tbl_6, tbl_7, tbl_8, tbl_9, tbl_10, tbl_11, tbl_12, tbl_13, tbl_14, tbl_15, tbl_16, tbl_17, tbl_18, tbl_19, tbl_20, tbl_21, tbl_22, tbl_23, tbl_24, tbl_25, W_top1, b_top1, W_top2, b_top2, W_top3)
    r_dense_features, ids, tbl_0, tbl_1, tbl_2, tbl_3, tbl_4, tbl_5, tbl_6, tbl_7, tbl_8, tbl_9, tbl_10, tbl_11, tbl_12, tbl_13, tbl_14, tbl_15, tbl_16, tbl_17, tbl_18, tbl_19, tbl_20, tbl_21, tbl_22, tbl_23, tbl_24, tbl_25, W_top1, b_top1, W_top2, b_top2, W_top3 = _rec_inputs()

    def _L0_rec_setup():
        import jax, jax.numpy as jnp
        import numpy as np
        F = 26
        N = F + 1
        _TRIU_I, _TRIU_J = np.triu_indices(N, k=1)
        key = jax.random.key(seed)
        k1, k2 = jax.random.split(key)
        B, D = (2048, 128)
        dense_features = jax.random.normal(k1, (B, D), dtype=jnp.float32)
        sparse_features = jax.random.normal(k2, (B, F, D), dtype=jnp.float32)
        return {'dense_features': dense_features, 'sparse_features': sparse_features}
    _L0_rec_all = _L0_rec_setup()
    _L0_rec_in = {k: v for k, v in _L0_rec_all.items() if k in ()}
    del _L0_rec_all
    return {'r_dense_features': r_dense_features, 'ids': ids, 'tbl_0': tbl_0, 'tbl_1': tbl_1, 'tbl_2': tbl_2, 'tbl_3': tbl_3, 'tbl_4': tbl_4, 'tbl_5': tbl_5, 'tbl_6': tbl_6, 'tbl_7': tbl_7, 'tbl_8': tbl_8, 'tbl_9': tbl_9, 'tbl_10': tbl_10, 'tbl_11': tbl_11, 'tbl_12': tbl_12, 'tbl_13': tbl_13, 'tbl_14': tbl_14, 'tbl_15': tbl_15, 'tbl_16': tbl_16, 'tbl_17': tbl_17, 'tbl_18': tbl_18, 'tbl_19': tbl_19, 'tbl_20': tbl_20, 'tbl_21': tbl_21, 'tbl_22': tbl_22, 'tbl_23': tbl_23, 'tbl_24': tbl_24, 'tbl_25': tbl_25, 'W_top1': W_top1, 'b_top1': b_top1, 'W_top2': W_top2, 'b_top2': b_top2, 'W_top3': W_top3}

def reference(r_dense_features, ids, tbl_0, tbl_1, tbl_2, tbl_3, tbl_4, tbl_5, tbl_6, tbl_7, tbl_8, tbl_9, tbl_10, tbl_11, tbl_12, tbl_13, tbl_14, tbl_15, tbl_16, tbl_17, tbl_18, tbl_19, tbl_20, tbl_21, tbl_22, tbl_23, tbl_24, tbl_25, W_top1, b_top1, W_top2, b_top2, W_top3):
    import jax
    import jax.numpy as jnp

    def _L0_rec_ref(dense_features, sparse_features):
        import jax, jax.numpy as jnp
        import numpy as np
        F = 26
        N = F + 1
        _TRIU_I, _TRIU_J = np.triu_indices(N, k=1)
        combined = jnp.concatenate([dense_features[:, None, :], sparse_features], axis=1)
        interactions = jnp.einsum('bnd,bmd->bnm', combined, combined)
        interactions_flat = interactions[:, _TRIU_I, _TRIU_J]
        return jnp.concatenate([dense_features, interactions_flat], axis=1)
    e = jnp.stack([tbl_0[ids[:, 0]], tbl_1[ids[:, 1]], tbl_2[ids[:, 2]], tbl_3[ids[:, 3]], tbl_4[ids[:, 4]], tbl_5[ids[:, 5]], tbl_6[ids[:, 6]], tbl_7[ids[:, 7]], tbl_8[ids[:, 8]], tbl_9[ids[:, 9]], tbl_10[ids[:, 10]], tbl_11[ids[:, 11]], tbl_12[ids[:, 12]], tbl_13[ids[:, 13]], tbl_14[ids[:, 14]], tbl_15[ids[:, 15]], tbl_16[ids[:, 16]], tbl_17[ids[:, 17]], tbl_18[ids[:, 18]], tbl_19[ids[:, 19]], tbl_20[ids[:, 20]], tbl_21[ids[:, 21]], tbl_22[ids[:, 22]], tbl_23[ids[:, 23]], tbl_24[ids[:, 24]], tbl_25[ids[:, 25]]], axis=1)
    z = _L0_rec_ref(r_dense_features, e)
    z = z.reshape(z.shape[0], -1)
    h = jnp.concatenate([z, r_dense_features], axis=1)
    h = jnp.maximum(h @ W_top1 + b_top1, 0.0)
    h = jnp.maximum(h @ W_top2 + b_top2, 0.0)
    y = h @ W_top3
    return y

_drawn_inputs = setup_inputs


def setup_inputs(seed=0):
    import zlib

    import numpy as np

    out = dict(_drawn_inputs(seed))
    spreads = {'b_top1': (0.0, 0.1), 'b_top2': (0.0, 0.1)}
    factors = {}
    for name, (base, spread) in spreads.items():
        noise = np.random.default_rng([zlib.crc32(name.encode()), seed]).standard_normal(out[name].shape)
        drawn = base * np.exp(spread * noise) if base else spread * noise
        out[name] = jnp.asarray(drawn.astype(out[name].dtype))
    for name, factor in factors.items():
        out[name] = (out[name] * factor).astype(out[name].dtype)
    return out
```

```python
from contextlib import ExitStack

import numpy as np

import concourse.bass as bass
from concourse import mybir

F32 = mybir.dt.float32
I32 = mybir.dt.int32
ALU = mybir.AluOpType
ACT = mybir.ActivationFunctionType

P = 128
TABLES = 26
N = TABLES + 1
B = 2048
TILE_COUNT = B // P
GROUP = 256
GROUPS = B // GROUP
TILES = GROUP // P
SLOTS = 2 * TILES
HALF = N // 2
UNITS = HALF + 1
CHUNKS = -(-UNITS // 4)
H1, H2 = 512, 256
H1_CHUNKS, H2_CHUNKS = H1 // P, H2 // P

BLOCK = 4
BLOCK_COLS = BLOCK * N
TILE_BLOCKS = P // BLOCK
GROUP_BLOCKS = GROUP // BLOCK
BANK_BLOCKS = 512 // BLOCK_COLS
ROUND_BLOCKS = 2 * BANK_BLOCKS
TILE_ROUNDS = TILE_BLOCKS // ROUND_BLOCKS
ROUNDS = TILES * TILE_ROUNDS
PER_BANK = 4
TILE_BANKS = -(-N // PER_BANK)
TRANSPOSE_USES = TILES * TILE_BANKS
MLP_USES = H1_CHUNKS + H2_CHUNKS + 1
WIDE = 32


def dlrm_tower(nc, dense, ids, tables, w1_dense, w1_again, w1_units, b1, w2, b2, w3, identity, late_rows, y):
    ctx = ExitStack()
    with ctx:
        def sb(name, shape, dtype):
            return ctx.enter_context(nc.sbuf_tensor(name, shape, dtype))

        def ps(name, shape):
            return ctx.enter_context(nc.psum_tensor(name, shape, F32))

        def sem(name):
            return ctx.enter_context(nc.semaphore(name))

        identity_sb = sb("identity_sb", [P, P], F32)
        late_sb = sb("late_sb", [P, HALF], I32)
        w1d_sb = sb("w1d_sb", [P, H1], F32)
        w1a_sb = sb("w1a_sb", [P, H1], F32)
        w1u_sb = sb("w1u_sb", [P, CHUNKS, H1], F32)
        w2_sb = sb("w2_sb", [P, H1_CHUNKS, H2], F32)
        w3_sb = sb("w3_sb", [P, H2_CHUNKS], F32)
        b1_sb = sb("b1_sb", [P, H1_CHUNKS], F32)
        b2_sb = sb("b2_sb", [P, H2_CHUNKS], F32)
        ids_sb = sb("ids_sb", [P, SLOTS, TABLES], I32)
        rows = sb("rows", [P, SLOTS, N, P], F32)
        embed_t = sb("embed_t", [P, SLOTS, P, WIDE], F32)
        units = sb("units", [P, UNITS, GROUP_BLOCKS], F32)
        packed = sb("packed", [P, CHUNKS, BLOCK, GROUP_BLOCKS], F32)
        hidden1 = sb("hidden1", [P, H1_CHUNKS, GROUP], F32)
        hidden2 = sb("hidden2", [P, H2_CHUNKS, GROUP], F32)
        y_sb = sb("y_sb", [1, B], F32)

        transpose_ps = ps("transpose_ps", [P, 2, PER_BANK, P])
        gram_ps = ps("gram_ps", [P, 4, 512])
        mlp_ps = ps("mlp_ps", [P, 2, 512])

        weights_loaded = sem("weights_loaded")
        const_loaded = sem("const_loaded")
        ids_loaded = [sem(f"ids_loaded{i}") for i in range(SLOTS)]
        gathered = [sem(f"gathered{i}") for i in range(SLOTS)]
        dense_loaded = [sem(f"dense_loaded{i}") for i in range(SLOTS)]
        padding_zeroed = sem("padding_zeroed")
        w1_summed = sem("w1_summed")
        gathers_begun = sem("gathers_begun")
        rounds_begun = sem("rounds_begun")
        transposed = sem("transposed")
        embed_even = sem("embed_even")
        embed_odd = sem("embed_odd")
        gram_ready = sem("gram_ready")
        late_copied = sem("late_copied")
        early_copied = sem("early_copied")
        units_packed = sem("units_packed")
        mlp_ready = sem("mlp_ready")
        mlp_copied = sem("mlp_copied")
        y_stored = sem("y_stored")
        PACK_DMAS = 16
        GATHERS = 16 * TABLES

        def features(u):
            return range(PER_BANK * u, min(N, PER_BANK * (u + 1)))

        def gram_slot(i):
            b = 2 * (i % 2)
            return gram_ps[:, b:b + 2, 0:BANK_BLOCKS * BLOCK_COLS].rearrange("p a (q s m) -> p a q s m", s=BLOCK, m=N)

        def unit_slot(s, r, first, last):
            at = units[32 * s:32 * s + 32, first:last, r * ROUND_BLOCKS:(r + 1) * ROUND_BLOCKS]
            return at.rearrange("p k (a q) -> p a q k", a=2)

        block = ctx.enter_context(nc.Block())

        @block.sync
        def _(sp):
            def load_tile(i, slot, first):
                t = SLOTS * i + slot
                if not first:
                    sp.wait_ge(gathered[slot], GATHERS * i)
                    sp.wait_ge(transposed, TILE_BANKS * (SLOTS * (i - 1) + slot + 1))
                sp.dma_start(ids_sb[:, slot, :], ids[bass.ds(t * P, P), :]).then_inc(ids_loaded[slot], 16)
                sp.dma_start(rows[:, slot, 0, :], dense[bass.ds(t * P, P), :]).then_inc(dense_loaded[slot], 16)

            def pack(g):
                sp.wait_ge(early_copied, ROUNDS * (g + 1))
                for s in range(BLOCK):
                    for j in range(4):
                        some = len(range(j, UNITS, 4))
                        sp.dma_start(packed[32 * j:32 * j + 32, 0:some, s, :],
                                     units[32 * s:32 * s + 32, j:UNITS:4, :]).then_inc(units_packed, 16)

            for slot in range(SLOTS):
                load_tile(0, slot, True)
            sp.dma_start(identity_sb[:, :], identity).then_inc(const_loaded, 16)
            sp.dma_start(late_sb[:, :], late_rows).then_inc(const_loaded, 16)
            sp.dma_start(w1d_sb[:, :], w1_dense).then_inc(weights_loaded, 16)
            sp.dma_start(w1a_sb[:, :], w1_again).then_inc(weights_loaded, 16)
            sp.dma_start(w1u_sb[:, 0:CHUNKS - 1, :],
                         w1_units[0:(CHUNKS - 1) * P, :].rearrange("(c p) h -> p c h", p=P)).then_inc(weights_loaded, 16)
            sp.dma_start(w1u_sb[0:64, CHUNKS - 1, :], w1_units[(CHUNKS - 1) * P:, :]).then_inc(weights_loaded, 16)
            sp.dma_start(b1_sb[:, :], b1).then_inc(weights_loaded, 16)
            sp.dma_start(w2_sb[:, :, :], w2.rearrange("(c p) h -> p c h", p=P)).then_inc(weights_loaded, 16)
            sp.dma_start(b2_sb[:, :], b2).then_inc(weights_loaded, 16)
            sp.dma_start(w3_sb[:, :], w3).then_inc(weights_loaded, 16)
            with sp.Fori(0, GROUPS // 2 - 1) as i:
                for half in range(2):
                    for slot in range(half * TILES, (half + 1) * TILES):
                        load_tile(i + 1, slot, False)
                    pack(2 * i + half)
            pack(GROUPS - 2)
            pack(GROUPS - 1)
            sp.wait_ge(mlp_copied, MLP_USES * GROUPS + 1)
            sp.dma_start(y.rearrange("(a b) c -> a (b c)", a=1), y_sb[0:1, :]).then_inc(y_stored, 16)
            sp.wait_ge(y_stored, 16)

        @block.gpsimd
        def _(pool):
            def gather(i, slot):
                pool.wait_ge(ids_loaded[slot], 16 * (i + 1))
                pool.sem_inc(gathers_begun, 1)
                for f in range(TABLES):
                    nc.gpsimd.indirect_dma_start(
                        rows[:, slot, 1 + f, :], None, tables[f],
                        bass.IndirectOffsetOnAxis(ids_sb[:, slot, f:f + 1], 0)).then_inc(gathered[slot], 16)

            with pool.Fori(0, TILE_COUNT // SLOTS) as i:
                for slot in range(SLOTS):
                    gather(i, slot)

        def copy_transposes(copy, t2, u, buf):
            f = features(u)
            bank = (t2 * TILE_BANKS + u) % 2
            out = embed_t[:, buf * TILES + t2, :, f[0]:f[-1] + 1].rearrange("p b n -> p n b")
            return copy(out, transpose_ps[:, bank, 0:len(f), :])

        @block.scalar
        def _(act):
            def embed_copies(g, buf):
                for v in range(TRANSPOSE_USES // 2):
                    use = 2 * v
                    act.wait_ge(transposed, TRANSPOSE_USES * g + use + 1)
                    copy_transposes(nc.scalar.copy, use // TILE_BANKS, use % TILE_BANKS, buf).then_inc(embed_even, 1)

            def mlp_copies(g):
                for m in range(MLP_USES):
                    act.wait_ge(mlp_ready, MLP_USES * g + m + 1)
                    src = mlp_ps[:, m % 2, 0:GROUP]
                    if m < H1_CHUNKS:
                        nc.scalar.activation(hidden1[:, m, :], src, ACT.Relu, bias=b1_sb[:, m:m + 1]).then_inc(mlp_copied, 1)
                    elif m < H1_CHUNKS + H2_CHUNKS:
                        c = m - H1_CHUNKS
                        nc.scalar.activation(hidden2[:, c, :], src, ACT.Relu, bias=b2_sb[:, c:c + 1]).then_inc(mlp_copied, 1)
                    else:
                        out = y_sb[0:1, bass.ds(g * GROUP, GROUP)].rearrange("p (q s) -> p s q", s=BLOCK)
                        nc.scalar.copy(out, src[0:1, :].rearrange("p (s q) -> p s q", s=BLOCK)).then_inc(mlp_copied, 1)

            def late_columns(g):
                for r in range(ROUNDS):
                    act.wait_ge(gram_ready, ROUNDS * g + r + 1)
                    for s in range(BLOCK):
                        last = nc.scalar.copy(unit_slot(s, r, 0, UNITS),
                                              gram_slot(r)[32 * s:32 * s + 32, :, :, s, HALF:N])
                    last.then_inc(late_copied, 1)

            act.sem_inc(mlp_copied, 1)
            act.wait_ge(weights_loaded, 16 * 8)
            embed_copies(0, 0)
            late_columns(0)
            with act.Fori(0, GROUPS // 2 - 1) as i:
                for half in range(2):
                    g = 2 * i + 1 + half
                    embed_copies(g, 1 - half)
                    mlp_copies(g - 1)
                    late_columns(g)
            embed_copies(GROUPS - 1, 1)
            mlp_copies(GROUPS - 2)
            late_columns(GROUPS - 1)
            mlp_copies(GROUPS - 1)

        @block.vector
        def _(dve):
            def embed_copies(g, buf):
                for v in range(TRANSPOSE_USES // 2):
                    use = 2 * v + 1
                    dve.wait_ge(transposed, TRANSPOSE_USES * g + use + 1)
                    copy_transposes(nc.vector.tensor_copy, use // TILE_BANKS, use % TILE_BANKS, buf).then_inc(embed_odd, 1)

            def early_columns(g):
                for r in range(ROUNDS):
                    dve.wait_ge(late_copied, ROUNDS * g + r + 1)
                    dve.sem_inc(rounds_begun, 1)
                    for s in range(BLOCK):
                        rows_taken = late_sb[32 * s:32 * s + 32, None, None, :].to_broadcast([32, 2, BANK_BLOCKS, HALF])
                        last = nc.vector.copy_predicated(unit_slot(s, r, 1, UNITS), rows_taken,
                                                         gram_slot(r)[32 * s:32 * s + 32, :, :, s, 0:HALF])
                    last.then_inc(early_copied, 1)

            dve.wait_ge(const_loaded, 32)
            for slot in range(SLOTS):
                last = nc.vector.memset(embed_t[:, slot, :, N:WIDE], 0.0)
            last.then_inc(padding_zeroed, 1)
            embed_copies(0, 0)
            dve.wait_ge(weights_loaded, 16 * 8)
            nc.vector.tensor_tensor(w1d_sb[:, :], w1d_sb[:, :], w1a_sb[:, :], ALU.add).then_inc(w1_summed, 1)
            early_columns(0)
            with dve.Fori(0, GROUPS // 2 - 1) as i:
                for half in range(2):
                    g = 2 * i + 1 + half
                    embed_copies(g, 1 - half)
                    early_columns(g)
            embed_copies(GROUPS - 1, 1)
            early_columns(GROUPS - 1)

        @block.tensor
        def _(pe):
            def transposes(pair, buf, first):
                g = 2 * pair + buf
                for t2 in range(TILES):
                    slot = buf * TILES + t2
                    pe.wait_ge(dense_loaded[slot], 16 * (pair + 1))
                    pe.wait_ge(gathered[slot], GATHERS * (pair + 1))
                    for u in range(TILE_BANKS):
                        use = t2 * TILE_BANKS + u
                        if not (first and use < 2):
                            pe.wait_ge((embed_even, embed_odd)[use % 2], TRANSPOSE_USES // 2 * g + use // 2)
                        for i, f in enumerate(features(u)):
                            last = nc.tensor.transpose(transpose_ps[:, use % 2, i, :], rows[:, slot, f, :], identity_sb[:, :])
                        last.then_inc(transposed, 1)

            def grams(g, buf, first):
                for r in range(ROUNDS):
                    if r % TILE_ROUNDS == 0:
                        done = (r // TILE_ROUNDS + 1) * TILE_BANKS
                        pe.wait_ge(embed_even, TRANSPOSE_USES // 2 * g + (done + 1) // 2)
                        pe.wait_ge(embed_odd, TRANSPOSE_USES // 2 * g + done // 2)
                    if not (first and r < 2):
                        pe.wait_ge(early_copied, ROUNDS * g + r - 1)
                    slot = buf * TILES + r // TILE_ROUNDS
                    for i in range(ROUND_BLOCKS):
                        b = (r % TILE_ROUNDS) * ROUND_BLOCKS + i
                        at = (i % BANK_BLOCKS) * BLOCK_COLS
                        last = nc.tensor.matmul(gram_ps[:, 2 * (r % 2) + i // BANK_BLOCKS, at:at + BLOCK_COLS],
                                                embed_t[:, slot, b * BLOCK:(b + 1) * BLOCK, :],
                                                embed_t[:, slot, b * BLOCK:(b + 1) * BLOCK, 0:N],
                                                start=True, stop=True)
                    last.then_inc(gram_ready, 1)

            def dense_columns(buf):
                whole = embed_t[:, buf * TILES:(buf + 1) * TILES, :, 0]
                return whole.rearrange("p t (q s) -> p s t q", s=BLOCK)

            def mlp(g, buf):
                pe.wait_ge(units_packed, 16 * PACK_DMAS * (g + 1))
                for m in range(MLP_USES):
                    out = mlp_ps[:, m % 2, 0:GROUP]
                    need = {H1_CHUNKS: H1_CHUNKS, H1_CHUNKS + H2_CHUNKS: H1_CHUNKS + H2_CHUNKS}.get(m, max(m - 1, 0))
                    pe.wait_ge(mlp_copied, MLP_USES * g + need + 1)
                    if m < H1_CHUNKS:
                        h = slice(m * P, (m + 1) * P)
                        for c in range(CHUNKS):
                            k = P if c < CHUNKS - 1 else 64
                            nc.tensor.matmul(out, w1u_sb[0:k, c, h], packed[0:k, c, :, :], start=(c == 0), stop=False)
                        last = nc.tensor.matmul(out, w1d_sb[:, h], dense_columns(buf), start=False, stop=True)
                    elif m < H1_CHUNKS + H2_CHUNKS:
                        h = slice((m - H1_CHUNKS) * P, (m - H1_CHUNKS + 1) * P)
                        for c in range(H1_CHUNKS):
                            last = nc.tensor.matmul(out, w2_sb[:, c, h], hidden1[:, c, :], start=(c == 0), stop=(c == H1_CHUNKS - 1))
                    else:
                        for c in range(H2_CHUNKS):
                            last = nc.tensor.matmul(out[0:1, :], w3_sb[:, c:c + 1], hidden2[:, c, :],
                                                    start=(c == 0), stop=(c == H2_CHUNKS - 1))
                    last.then_inc(mlp_ready, 1)

            pe.wait_ge(const_loaded, 32)
            transposes(0, 0, True)
            pe.wait_ge(padding_zeroed, 1)
            grams(0, 0, True)
            pe.wait_ge(w1_summed, 1)
            pe.wait_ge(weights_loaded, 16 * 8)
            with pe.Fori(0, GROUPS // 2 - 1) as i:
                for half in range(2):
                    g, buf = 2 * i + 1 + half, 1 - half
                    transposes(i + half, buf, False)
                    mlp(g - 1, 1 - buf)
                    grams(g, buf, False)
            transposes(GROUPS // 2 - 1, 1, False)
            mlp(GROUPS - 2, 0)
            grams(GROUPS - 1, 1, False)
            mlp(GROUPS - 1, 1)


def unit_rows():
    def pair(i, j):
        i, j = min(i, j), max(i, j)
        return P + i * N - i * (i + 1) // 2 + (j - i - 1)

    seen, rows = set(), -np.ones((UNITS, 32), int)
    for k in range(UNITS):
        for n in range(N):
            m = k - 1 if k and k <= n < k + HALF else HALF + k
            if n != m and pair(n, m) not in seen:
                seen.add(pair(n, m))
                rows[k, n] = pair(n, m)
    assert len(seen) == N * (N - 1) // 2
    return rows.reshape(-1)


def by_partition(x):
    return np.ascontiguousarray(x.reshape(-1, P).T)


def kernel(**inputs):
    import concourse.bacc as bacc
    from concourse.bass_utils import run_bass_kernel_spmd

    a = {name: np.asarray(x) for name, x in inputs.items()}
    pairs = P + N * (N - 1) // 2
    w1 = a["W_top1"]
    where = unit_rows()
    w1_units = np.zeros((UNITS * 32, H1), w1.dtype)
    w1_units[where >= 0] = w1[where[where >= 0]]
    late = np.zeros((BLOCK, 32, HALF), np.int32)
    for k in range(1, UNITS):
        late[:, k:k + HALF, k - 1] = 1
    given = {
        "dense": a["r_dense_features"], "ids": a["ids"],
        **{f"table{f}": a[f"tbl_{f}"] for f in range(TABLES)},
        "w1_dense": np.ascontiguousarray(w1[0:P]), "w1_again": np.ascontiguousarray(w1[pairs:]), "w1_units": w1_units,
        "b1": by_partition(a["b_top1"]), "w2": a["W_top2"], "b2": by_partition(a["b_top2"]), "w3": by_partition(a["W_top3"]),
        "identity": np.eye(P, dtype=np.float32), "late_rows": late.reshape(P, HALF),
    }
    nc = bacc.Bacc("TRN2", target_bir_lowering=False, num_devices=1)
    aps = {n: nc.dram_tensor(n, x.shape, mybir.dt.from_np(x.dtype), kind="ExternalInput").ap() for n, x in given.items()}
    y = nc.dram_tensor("y", (B, 1), F32, kind="ExternalOutput").ap()
    tables = [aps.pop(f"table{f}") for f in range(TABLES)]
    dlrm_tower(nc, tables=tables, y=y, **aps)
    result = run_bass_kernel_spmd(nc, [given], core_ids=[0])
    return result.results[0]["y"]
```

```python
from contextlib import ExitStack

import numpy as np

import concourse.bass as bass
from concourse import mybir

F32 = mybir.dt.float32
F32R = mybir.dt.float32r
I32 = mybir.dt.int32
ALU = mybir.AluOpType
ACT = mybir.ActivationFunctionType

P = 128
TABLES = 26
N = TABLES + 1
B = 2048
HOT_ROWS = 1000
HOT = 7
ROWS = [1000, 125000, 12500, 1250, 12500, 1000, 1250, 1000, 1000, 1000, 12500, 1000, 1250, 1250, 1250, 1000, 1000,
        12500, 1250, 1250, 1000, 1000, 1250, 1000, 1250, 12500]
HOT_TABLES = [f for f in range(TABLES) if ROWS[f] == HOT_ROWS][:HOT]
GATHERED_TABLES = [f for f in range(TABLES) if f not in HOT_TABLES]
GATHERED = len(GATHERED_TABLES)
FEATURES = [0] + [1 + f for f in GATHERED_TABLES + HOT_TABLES]
HOT_FEATURE = 1 + GATHERED
HOT_P = 125
HOT_STEPS = HOT_ROWS // HOT_P
TILE_COUNT = B // P
GROUP = 256
GROUPS = B // GROUP
TILES = GROUP // P
SLOTS = 2 * TILES
HALF = N // 2
UNITS = HALF + 1
CHUNKS = 3
UNIT_P = UNITS * N // CHUNKS
H1, H2 = 512, 256
H1_CHUNKS, H2_CHUNKS = H1 // P, H2 // P

BLOCK = 4
BLOCK_COLS = BLOCK * N
TILE_BLOCKS = P // BLOCK
GROUP_BLOCKS = GROUP // BLOCK
BANK_BLOCKS = 512 // BLOCK_COLS
ROUND_BLOCKS = BANK_BLOCKS
TILE_ROUNDS = TILE_BLOCKS // ROUND_BLOCKS
ROUNDS = TILES * TILE_ROUNDS
PER_BANK = 4
TILE_BANKS = -(-HOT_FEATURE // PER_BANK)
TRANSPOSE_USES = TILES * TILE_BANKS
MLP_USES = H1_CHUNKS + H2_CHUNKS + 1

STEPS = [
    "B0 G0 Q0 G1 Q1 H0 G2 Q2 H1 G3 M0 G4 M1 Q3 M2 G5 M3 H2 M4 G6 M5 Q4 G7 M6".split(),
    "G0 Q0 H3 G1 Q1 G2 H4 Q2 G3 G4 H5 Q3 G5 G6 Q4 G7 H6".split(),
]
LAST_STEPS = [
    "G0 G1 G2 G3 G4 G5 M0 G6 M1 G7 M2 M3 Q0 M4 Q1 M5 Q2 M6 Q3 Q4".split(),
    "G0 G1 G2 G3 G4 G5 G6 G7".split(),
]
FIRST_STEPS = "H0 H1 Q0 H2 Q1 H3 Q2 H4 Q3 H5 Q4 H6".split()
WIDE = 32


def dlrm_tower(nc, dense, ids, hot_ids, row_numbers, tables, w1_dense, w1_again, w1_units, b1, w2, b2, w3, identity, late_rows, bounce, y):
    ctx = ExitStack()
    with ctx:
        def sb(name, shape, dtype):
            return ctx.enter_context(nc.sbuf_tensor(name, shape, dtype))

        def ps(name, shape):
            return ctx.enter_context(nc.psum_tensor(name, shape, F32))

        def sem(name):
            return ctx.enter_context(nc.semaphore(name))

        identity_sb = sb("identity_sb", [P, P], F32)
        late_sb = sb("late_sb", [P, HALF], I32)
        w1d_sb = sb("w1d_sb", [P, H1], F32)
        w1u_sb = sb("w1u_sb", [UNIT_P, CHUNKS, H1], F32)
        w2_sb = sb("w2_sb", [P, H1_CHUNKS, H2], F32)
        w3_sb = sb("w3_sb", [P, H2_CHUNKS], F32)
        b1_sb = sb("b1_sb", [P, H1_CHUNKS], F32)
        b2_sb = sb("b2_sb", [P, H2_CHUNKS], F32)
        ids_sb = sb("ids_sb", [P, SLOTS, TABLES], I32)
        rows = sb("rows", [P, TILES, HOT_FEATURE, P], F32)
        hot_ids_sb = sb("hot_ids_sb", [P, B], F32R)
        selector = sb("selector", [P, HOT, HOT_P], F32R)
        row_numbers_sb = sb("row_numbers_sb", [HOT_P, HOT_STEPS], F32)
        table_hi = sb("table_hi", [HOT_P, HOT, HOT_STEPS, P], F32R)
        table_lo = sb("table_lo", [HOT_P, HOT, HOT_STEPS, P], F32R)
        one_hot = sb("one_hot", [HOT_P, 2, HOT_STEPS, GROUP], F32R)
        embed_t = sb("embed_t", [P, SLOTS, P, WIDE], F32)
        units = sb("units", [P, 2, UNITS, GROUP_BLOCKS], F32)
        packed = sb("packed", [UNIT_P, CHUNKS, GROUP], F32)
        hidden1 = sb("hidden1", [P, H1_CHUNKS, GROUP], F32)
        hidden2 = sb("hidden2", [P, H2_CHUNKS, GROUP], F32)
        y_sb = sb("y_sb", [1, 2, GROUP], F32)

        raw_tables = [units[0:HOT_P].rearrange("p a k q -> p (a k q)")[:, 0:HOT_STEPS * P].rearrange("p (j d) -> p j d", d=P),
                      hidden1[0:HOT_P].rearrange("p c b -> p (c b)").rearrange("p (j d) -> p j d", d=P)]

        w1a_sb = hidden2[:, :, :].rearrange("p c b -> p (c b)")

        transpose_ps = ps("transpose_ps", [P, 2, PER_BANK, P])
        gram_ps = ps("gram_ps", [P, 2, 512])
        hot_ids_ps = ps("hot_ids_ps", [P, 512])
        hot_ps = ps("hot_ps", [P, 512])
        mlp_ps = ps("mlp_ps", [P, 2, 512])

        weights_loaded = sem("weights_loaded")
        const_loaded = sem("const_loaded")
        ids_loaded = [sem(f"ids_loaded{i}") for i in range(SLOTS)]
        gathered = [[sem(f"gathered{i}_{u}") for u in range(TILE_BANKS)] for i in range(TILES)]
        dense_loaded = [sem(f"dense_loaded{i}") for i in range(TILES)]
        raw_loaded = [sem(f"raw_loaded{i}") for i in range(2)]
        hi_split = sem("hi_split")
        lo_split = sem("lo_split")
        hot_ids_zeroed = sem("hot_ids_zeroed")
        hot_ids_loaded = sem("hot_ids_loaded")
        selector_ready = sem("selector_ready")
        hot_ids_ready = sem("hot_ids_ready")
        one_hot_ready = sem("one_hot_ready")
        hot_ready = sem("hot_ready")
        hot_copied = sem("hot_copied")
        padding_zeroed = sem("padding_zeroed")
        w1_summed = sem("w1_summed")
        gathers_begun = sem("gathers_begun")
        rounds_begun = sem("rounds_begun")
        stores_begun = sem("stores_begun")
        transposed = sem("transposed")
        embed_even = sem("embed_even")
        embed_odd = sem("embed_odd")
        gram_ready = sem("gram_ready")
        late_copied = sem("late_copied")
        early_copied = sem("early_copied")
        units_stored = sem("units_stored")
        units_packed = sem("units_packed")
        mlp_ready = sem("mlp_ready")
        mlp_copied = sem("mlp_copied")
        y_stored = sem("y_stored")

        def features(u):
            return range(PER_BANK * u, min(HOT_FEATURE, PER_BANK * (u + 1)))

        def gathers(u):
            return [f for f in features(u) if f > 0]

        def gram_slot(i):
            return gram_ps[:, i % 2, 0:BANK_BLOCKS * BLOCK_COLS].rearrange("p (q s m) -> p q s m", s=BLOCK, m=N)

        def unit_slot(buf, s, r, first, last):
            at = units[32 * s:32 * s + 32, buf, first:last, r * ROUND_BLOCKS:(r + 1) * ROUND_BLOCKS]
            return at.rearrange("p k q -> p q k")

        block = ctx.enter_context(nc.Block())

        @block.sync
        def _(sp):
            def load_ids(t, slot):
                sp.dma_start(ids_sb[:, slot, :], ids[bass.ds(t * P, P), :]).then_inc(ids_loaded[slot], 16)

            def load_dense(t, t2):
                sp.dma_start(rows[:, t2, 0, :], dense[bass.ds(t * P, P), :]).then_inc(dense_loaded[t2], 16)

            def load_hot_table(k):
                if k >= 2:
                    sp.wait_ge(lo_split, k - 1)
                sp.dma_start(raw_tables[k % 2], tables[HOT_TABLES[k]].rearrange("(p j) d -> p j d", p=HOT_P)).then_inc(
                    raw_loaded[k % 2], 16)

            def pack(g, buf):
                sp.wait_ge(early_copied, ROUNDS * (g + 1))
                for s in range(BLOCK):
                    sp.dma_start(bounce.rearrange("(n k) (s q) -> s n k q", n=N, s=BLOCK)[s],
                                 units[32 * s:32 * s + N, buf, :, :]).then_inc(units_stored, 16)
                sp.wait_ge(units_stored, 16 * BLOCK * (g + 1))
                sp.dma_start(packed[:, :, :], bounce.rearrange("(p c) b -> p c b", c=CHUNKS)).then_inc(units_packed, 16)

            def store_y(g, buf):
                sp.wait_ge(mlp_copied, MLP_USES * (g + 1) + 1)
                sp.dma_start(y[bass.ds(g * GROUP, GROUP), :].rearrange("(a b) c -> a (b c)", a=1),
                             y_sb[0:1, buf, :]).then_inc(y_stored, 16)

            def group(g, buf, loads=(True, True), stores=True, stored=True):
                for t2 in range(TILES):
                    if loads[0]:
                        sp.wait_ge(transposed, TRANSPOSE_USES * g + TILE_BANKS * (t2 + 1))
                        load_dense(TILES * (g + 1) + t2, t2)
                    if loads[1]:
                        load_ids(TILES * (g + 2) + t2, buf * TILES + t2)
                if stored:
                    sp.wait_ge(y_stored, 16 * (g - 1))
                    sp.sem_inc(stores_begun, 1)
                pack(g, buf)
                if stores:
                    store_y(g - 1, 1 - buf)

            load_ids(0, 0)
            sp.dma_start(identity_sb[:, :], identity).then_inc(const_loaded, 16)
            sp.dma_start(row_numbers_sb[:, :], row_numbers).then_inc(const_loaded, 16)
            load_hot_table(0)
            load_hot_table(1)
            for slot in range(1, SLOTS):
                load_ids(slot, slot)
            for t2 in range(TILES):
                load_dense(t2, t2)
            sp.dma_start(late_sb[:, :], late_rows).then_inc(const_loaded, 16)
            for k in range(2, HOT):
                load_hot_table(k)
            sp.dma_start(w1d_sb[:, :], w1_dense).then_inc(weights_loaded, 16)
            sp.dma_start(w1a_sb, w1_again).then_inc(weights_loaded, 16)
            sp.dma_start(w1u_sb[:, :, :], w1_units.rearrange("(p c) h -> p c h", c=CHUNKS)).then_inc(weights_loaded, 16)
            sp.dma_start(b1_sb[:, :], b1).then_inc(weights_loaded, 16)
            sp.dma_start(w2_sb[:, :, :], w2.rearrange("(c p) h -> p c h", p=P)).then_inc(weights_loaded, 16)
            sp.dma_start(b2_sb[:, :], b2).then_inc(weights_loaded, 16)
            sp.dma_start(w3_sb[:, :], w3).then_inc(weights_loaded, 16)
            group(0, 0, stores=False, stored=False)
            group(1, 1, stored=False)
            with sp.Fori(1, GROUPS // 2 - 1) as i:
                group(2 * i, 0)
                group(2 * i + 1, 1)
            group(GROUPS - 2, 0, loads=(True, False))
            group(GROUPS - 1, 1, loads=(False, False))
            store_y(GROUPS - 1, 1)
            sp.wait_ge(y_stored, 16 * GROUPS)

        @block.gpsimd
        def _(pool):
            def gather(i, slot, first, between=None):
                t2 = slot % TILES
                pool.wait_ge(ids_loaded[slot], 16 * (i + 1))
                if first is False and slot >= 0:
                    pool.sem_inc(gathers_begun, 1)
                for u in range(TILE_BANKS):
                    if not first:
                        pool.wait_ge(transposed, TILE_BANKS * (SLOTS * i + slot - TILES) + u + 1)
                        pool.sem_inc(gathers_begun, 1)
                    for f in gathers(u):
                        table = GATHERED_TABLES[f - 1]
                        nc.gpsimd.indirect_dma_start(
                            rows[:, t2, f, :], None, tables[table],
                            bass.IndirectOffsetOnAxis(ids_sb[:, slot, table:table + 1], 0)).then_inc(gathered[t2][u], 16)

            pool.wait_ge(hot_ids_zeroed, 1)
            nc.gpsimd.dma_start(hot_ids_sb[0:HOT, :], hot_ids).then_inc(hot_ids_loaded, 16)
            for slot in range(SLOTS):
                gather(0, slot, slot < TILES)
            with pool.Fori(1, TILE_COUNT // SLOTS) as i:
                for slot in range(SLOTS):
                    gather(i, slot, False)

        def next_tile(g, buf, t2):
            return (g, buf, 1) if t2 == 0 else (g + 1, 1 - buf, 0)

        def copy_transposes(copy, t2, u, buf):
            f = features(u)
            bank = (t2 * TILE_BANKS + u) % 2
            out = embed_t[:, buf * TILES + t2, :, f[0]:f[-1] + 1].rearrange("p b n -> p n b")
            return copy(out, transpose_ps[:, bank, 0:len(f), :])

        @block.scalar
        def _(act):
            def embed_copy(g, buf, t2, u):
                use = t2 * TILE_BANKS + u
                if use % 2 == 0:
                    act.wait_ge(transposed, TRANSPOSE_USES * g + use + 1)
                    copy_transposes(nc.scalar.copy, t2, u, buf).then_inc(embed_even, 1)

            def mlp_copy(g, buf, m):
                act.wait_ge(mlp_ready, MLP_USES * g + m + 1)
                src = mlp_ps[:, m % 2, 0:GROUP]
                if m < H1_CHUNKS:
                    nc.scalar.activation(hidden1[:, m, :], src, ACT.Relu, bias=b1_sb[:, m:m + 1]).then_inc(mlp_copied, 1)
                elif m < H1_CHUNKS + H2_CHUNKS:
                    c = m - H1_CHUNKS
                    nc.scalar.activation(hidden2[:, c, :], src, ACT.Relu, bias=b2_sb[:, c:c + 1]).then_inc(mlp_copied, 1)
                else:
                    out = y_sb[0:1, buf, :].rearrange("p (q s) -> p s q", s=BLOCK)
                    nc.scalar.copy(out, src[0:1, :].rearrange("p (s q) -> p s q", s=BLOCK)).then_inc(mlp_copied, 1)

            def late_columns(g, buf, r):
                act.wait_ge(gram_ready, ROUNDS * g + r + 1)
                for s in range(BLOCK):
                    last = nc.scalar.copy(unit_slot(buf, s, r, 0, UNITS), gram_slot(r)[32 * s:32 * s + 32, :, s, HALF:N])
                last.then_inc(late_copied, 1)

            def hot_copy(g, k, buf):
                act.wait_ge(hot_ready, HOT * g + k + 1)
                out = embed_t[:, buf * TILES:(buf + 1) * TILES, :, HOT_FEATURE + k]
                nc.scalar.copy(out, hot_ps[:, 0:GROUP].rearrange("p (t b) -> p t b", t=TILES)).then_inc(hot_copied, 1)

            def group(g, buf, steps, mlp_before=True):
                for t2 in range(TILES):
                    for step, n in [(x[0], int(x[1:])) for x in steps[t2]]:
                        if step == "G":
                            late_columns(g, buf, t2 * TILE_ROUNDS + n)
                        elif step == "Q":
                            embed_copy(*next_tile(g, buf, t2), n)
                        elif step == "H":
                            hot_copy(g + 1, n, 1 - buf)
                        elif step == "M" and mlp_before:
                            mlp_copy(g - 1, 1 - buf, n)

            act.sem_inc(mlp_copied, 1)

            def split_hi(k):
                act.wait_ge(raw_loaded[k % 2], 16 * (k // 2 + 1))
                nc.scalar.copy(table_hi[:, k], raw_tables[k % 2]).then_inc(hi_split, 1)

            split_hi(0)
            for step, n in [(x[0], int(x[1:])) for x in FIRST_STEPS]:
                if step == "H":
                    if n + 1 < HOT:
                        split_hi(n + 1)
                    hot_copy(0, n, 0)
                else:
                    embed_copy(0, 0, 0, n)
            group(0, 0, STEPS, False)
            act.wait_ge(weights_loaded, 16 * 7)
            with act.Fori(0, GROUPS // 2 - 1) as i:
                group(2 * i + 1, 1, STEPS)
                group(2 * i + 2, 0, STEPS)
            group(GROUPS - 1, 1, LAST_STEPS)
            for m in range(MLP_USES):
                mlp_copy(GROUPS - 1, 1, m)

        @block.vector
        def _(dve):
            def embed_copy(g, buf, t2, u):
                use = t2 * TILE_BANKS + u
                if use % 2 == 1:
                    dve.wait_ge(transposed, TRANSPOSE_USES * g + use + 1)
                    copy_transposes(nc.vector.tensor_copy, t2, u, buf).then_inc(embed_odd, 1)

            def early_columns(g, buf, r):
                dve.wait_ge(late_copied, ROUNDS * g + r + 1)
                dve.sem_inc(rounds_begun, 1)
                for s in range(BLOCK):
                    rows_taken = late_sb[32 * s:32 * s + 32, None, :].to_broadcast([32, BANK_BLOCKS, HALF])
                    last = nc.vector.copy_predicated(unit_slot(buf, s, r, 1, UNITS), rows_taken,
                                                     gram_slot(r)[32 * s:32 * s + 32, :, s, 0:HALF])
                last.then_inc(early_copied, 1)

            def make_one_hot(g, k, buf, first=False):
                i = HOT * g + k
                if not first:
                    dve.wait_ge(hot_ready, i - 1)
                dve.wait_ge(hot_ids_ready, i + 1)
                ids_over = hot_ids_ps[0:HOT_P, None, 0:GROUP].to_broadcast([HOT_P, HOT_STEPS, GROUP])
                numbers_over = row_numbers_sb[:, :, None].to_broadcast([HOT_P, HOT_STEPS, GROUP])
                nc.vector.tensor_tensor(one_hot[:, (HOT * buf + k) % 2], ids_over, numbers_over, ALU.is_equal).then_inc(
                    one_hot_ready, 1)

            def split_lo(k):
                dve.wait_ge(hi_split, k + 1)
                nc.vector.tensor_tensor(table_lo[:, k], raw_tables[k % 2], table_hi[:, k].bitcast(F32),
                                        ALU.subtract).then_inc(lo_split, 1)

            def group(g, buf, steps):
                for t2 in range(TILES):
                    for step, n in [(x[0], int(x[1:])) for x in steps[t2]]:
                        if step == "G":
                            early_columns(g, buf, t2 * TILE_ROUNDS + n)
                        elif step == "Q":
                            embed_copy(*next_tile(g, buf, t2), n)
                        elif step == "B":
                            make_one_hot(g + 1, 0, 1 - buf)
                        elif step == "H" and n + 1 < HOT:
                            make_one_hot(g + 1, n + 1, 1 - buf)

            nc.vector.memset(hot_ids_sb[:, :].bitcast(F32), 0.0).then_inc(hot_ids_zeroed, 1)
            dve.wait_ge(const_loaded, 16 * 3)
            nc.vector.tensor_copy(selector[:, :, :], identity_sb[:, 0:HOT, None].to_broadcast([P, HOT, HOT_P])).then_inc(
                selector_ready, 1)
            make_one_hot(0, 0, 0, True)
            split_lo(0)
            for step, n in [(x[0], int(x[1:])) for x in FIRST_STEPS]:
                if step == "H" and n + 1 < HOT:
                    make_one_hot(0, n + 1, 0, n == 0)
                    split_lo(n + 1)
                elif step == "Q":
                    embed_copy(0, 0, 0, n)
            for slot in range(SLOTS):
                last = nc.vector.memset(embed_t[:, slot, :, N:WIDE], 0.0)
            last.then_inc(padding_zeroed, 1)
            group(0, 0, STEPS)
            dve.wait_ge(weights_loaded, 16 * 7)
            nc.vector.tensor_tensor(w1d_sb[:, :], w1d_sb[:, :], w1a_sb, ALU.add).then_inc(w1_summed, 1)
            with dve.Fori(0, GROUPS // 2 - 1) as i:
                group(2 * i + 1, 1, STEPS)
                group(2 * i + 2, 0, STEPS)
            group(GROUPS - 1, 1, LAST_STEPS)

        @block.tensor
        def _(pe):
            def transposes(g, buf, t2, u, first=False):
                use = t2 * TILE_BANKS + u
                if u == 0:
                    pe.wait_ge(dense_loaded[t2], 16 * (g + 1))
                pe.wait_ge(gathered[t2][u], 16 * len(gathers(u)) * (g + 1))
                if not (first and use < 2):
                    pe.wait_ge((embed_even, embed_odd)[use % 2], TRANSPOSE_USES // 2 * g + use // 2)
                for i, f in enumerate(features(u)):
                    last = nc.tensor.transpose(transpose_ps[:, use % 2, i, :], rows[:, t2, f, :], identity_sb[:, :])
                last.then_inc(transposed, 1)

            def broadcast_ids(g, k):
                nc.tensor.matmul(hot_ids_ps[0:HOT_P, 0:GROUP], selector[:, k, :], hot_ids_sb[:, bass.ds(g * GROUP, GROUP)],
                                 start=True, stop=True).then_inc(hot_ids_ready, 1)

            def look_up(g, k, buf, first=False):
                i = HOT * g + k
                pe.wait_ge(one_hot_ready, i + 1)
                if k + 1 < HOT:
                    broadcast_ids(g, k + 1)
                if first:
                    pe.wait_ge(lo_split, k + 1)
                if not (first and k == 0):
                    pe.wait_ge(hot_copied, i)
                parts = [(table, j) for j in range(HOT_STEPS) for table in (table_hi, table_lo)]
                for table, j in parts:
                    last = nc.tensor.matmul(hot_ps[:, 0:GROUP], table[:, k, j, :], one_hot[:, (HOT * buf + k) % 2, j, :],
                                            start=(j == 0 and table is table_hi),
                                            stop=(j == HOT_STEPS - 1 and table is table_lo))
                last.then_inc(hot_ready, 1)

            def gram(g, buf, t2, n, first):
                r = t2 * TILE_ROUNDS + n
                if n == 0:
                    done = (t2 + 1) * TILE_BANKS
                    pe.wait_ge(embed_even, TRANSPOSE_USES // 2 * g + (done + 1) // 2)
                    pe.wait_ge(embed_odd, TRANSPOSE_USES // 2 * g + done // 2)
                    pe.wait_ge(hot_copied, HOT * (g + 1))
                if not (first and r < 2):
                    pe.wait_ge(early_copied, ROUNDS * g + r - 1)
                slot = buf * TILES + t2
                for i in range(ROUND_BLOCKS):
                    b = n * ROUND_BLOCKS + i
                    last = nc.tensor.matmul(gram_ps[:, r % 2, i * BLOCK_COLS:(i + 1) * BLOCK_COLS],
                                            embed_t[:, slot, b * BLOCK:(b + 1) * BLOCK, :],
                                            embed_t[:, slot, b * BLOCK:(b + 1) * BLOCK, 0:N],
                                            start=True, stop=True)
                last.then_inc(gram_ready, 1)

            def dense_columns(buf):
                whole = embed_t[:, buf * TILES:(buf + 1) * TILES, :, 0]
                return whole.rearrange("p t (q s) -> p s t q", s=BLOCK)

            def mlp(g, buf, m):
                out = mlp_ps[:, m % 2, 0:GROUP]
                need = {H1_CHUNKS: H1_CHUNKS, H1_CHUNKS + H2_CHUNKS: H1_CHUNKS + H2_CHUNKS}.get(m, max(m - 1, 0))
                pe.wait_ge(mlp_copied, MLP_USES * g + need + 1)
                if m < H1_CHUNKS:
                    h = slice(m * P, (m + 1) * P)
                    nc.tensor.matmul(out, w1d_sb[:, h], dense_columns(buf), start=True, stop=False)
                    if m == 0:
                        pe.wait_ge(units_packed, 16 * (g + 1))
                    for c in range(CHUNKS):
                        last = nc.tensor.matmul(out, w1u_sb[:, c, h], packed[:, c, :], start=False, stop=(c == CHUNKS - 1))
                elif m < H1_CHUNKS + H2_CHUNKS:
                    h = slice((m - H1_CHUNKS) * P, (m - H1_CHUNKS + 1) * P)
                    for c in range(H1_CHUNKS):
                        last = nc.tensor.matmul(out, w2_sb[:, c, h], hidden1[:, c, :], start=(c == 0), stop=(c == H1_CHUNKS - 1))
                else:
                    for c in range(H2_CHUNKS):
                        last = nc.tensor.matmul(out[0:1, :], w3_sb[:, c:c + 1], hidden2[:, c, :],
                                                start=(c == 0), stop=(c == H2_CHUNKS - 1))
                last.then_inc(mlp_ready, 1)

            def group(g, buf, steps, first=False):
                for t2 in range(TILES):
                    for step, n in [(x[0], int(x[1:])) for x in steps[t2]]:
                        if step == "G":
                            gram(g, buf, t2, n, first)
                        elif step == "Q":
                            transposes(*next_tile(g, buf, t2), n)
                        elif step == "B":
                            broadcast_ids(g + 1, 0)
                        elif step == "H":
                            look_up(g + 1, n, 1 - buf)
                        elif step == "M" and not first:
                            mlp(g - 1, 1 - buf, n)

            pe.wait_ge(const_loaded, 16 * 3)
            pe.wait_ge(selector_ready, 1)
            pe.wait_ge(hot_ids_loaded, 16)
            broadcast_ids(0, 0)
            for step, n in [(x[0], int(x[1:])) for x in FIRST_STEPS]:
                if step == "H":
                    look_up(0, n, 0, first=True)
                else:
                    transposes(0, 0, 0, n, first=True)
            pe.wait_ge(padding_zeroed, 1)
            group(0, 0, STEPS, first=True)
            pe.wait_ge(w1_summed, 1)
            pe.wait_ge(weights_loaded, 16 * 7)
            with pe.Fori(0, GROUPS // 2 - 1) as i:
                group(2 * i + 1, 1, STEPS)
                group(2 * i + 2, 0, STEPS)
            group(GROUPS - 1, 1, LAST_STEPS)
            for m in range(MLP_USES):
                mlp(GROUPS - 1, 1, m)


def unit_rows():
    def pair(i, j):
        i, j = min(i, j), max(i, j)
        return P + i * N - i * (i + 1) // 2 + (j - i - 1)

    seen, rows = set(), -np.ones((N, UNITS), int)
    for k in range(UNITS):
        for n in range(N):
            m = k - 1 if k and k <= n < k + HALF else HALF + k
            row = pair(FEATURES[n], FEATURES[m]) if n != m else -1
            if row not in seen | {-1}:
                seen.add(row)
                rows[n, k] = row
    assert len(seen) == N * (N - 1) // 2
    return rows.reshape(-1)


def by_partition(x):
    return np.ascontiguousarray(x.reshape(-1, P).T)


def kernel(**inputs):
    import concourse.bacc as bacc
    from concourse.bass_utils import run_bass_kernel_spmd

    a = {name: np.asarray(x) for name, x in inputs.items()}
    pairs = P + N * (N - 1) // 2
    w1 = a["W_top1"]
    where = unit_rows()
    w1_units = np.zeros((UNITS * N, H1), w1.dtype)
    w1_units[where >= 0] = w1[where[where >= 0]]
    late = np.zeros((BLOCK, 32, HALF), np.int32)
    for k in range(1, UNITS):
        late[:, k:k + HALF, k - 1] = 1
    given = {
        "dense": a["r_dense_features"], "ids": a["ids"], "hot_ids": np.ascontiguousarray(a["ids"].T[HOT_TABLES]),
        "row_numbers": np.arange(HOT_ROWS, dtype=np.float32).reshape(HOT_P, HOT_STEPS),
        **{f"table{f}": a[f"tbl_{f}"] for f in range(TABLES)},
        "w1_dense": np.ascontiguousarray(w1[0:P]), "w1_again": np.ascontiguousarray(w1[pairs:]), "w1_units": w1_units,
        "b1": by_partition(a["b_top1"]), "w2": a["W_top2"], "b2": by_partition(a["b_top2"]), "w3": by_partition(a["W_top3"]),
        "identity": np.eye(P, dtype=np.float32), "late_rows": late.reshape(P, HALF),
    }
    nc = bacc.Bacc("TRN2", target_bir_lowering=False, num_devices=1)
    aps = {n: nc.dram_tensor(n, x.shape, mybir.dt.from_np(x.dtype), kind="ExternalInput").ap() for n, x in given.items()}
    y = nc.dram_tensor("y", (B, 1), F32, kind="ExternalOutput").ap()
    bounce = nc.dram_tensor("bounce", (UNITS * N, GROUP), F32, kind="Internal").ap()
    tables = [aps.pop(f"table{f}") for f in range(TABLES)]
    dlrm_tower(nc, tables=tables, bounce=bounce, y=y, **aps)
    result = run_bass_kernel_spmd(nc, [given], core_ids=[0])
    return result.results[0]["y"]
```

```python
from contextlib import ExitStack

import numpy as np

import concourse.bass as bass
from concourse import mybir

F32 = mybir.dt.float32
F32R = mybir.dt.float32r
F16 = mybir.dt.float16
I32 = mybir.dt.int32
ALU = mybir.AluOpType
ACT = mybir.ActivationFunctionType

P = 128
TABLES = 26
N = TABLES + 1
B = 2048
HOT_ROWS = 1000
HOT = 8
ROWS = [1000, 125000, 12500, 1250, 12500, 1000, 1250, 1000, 1000, 1000, 12500, 1000, 1250, 1250, 1250, 1000, 1000,
        12500, 1250, 1250, 1000, 1000, 1250, 1000, 1250, 12500]
HOT_TABLES = [f for f in range(TABLES) if ROWS[f] == HOT_ROWS][:HOT]
GATHERED_TABLES = [f for f in range(TABLES) if f not in HOT_TABLES]
GATHERED = len(GATHERED_TABLES)
FEATURES = [0] + [1 + f for f in GATHERED_TABLES + HOT_TABLES]
HOT_FEATURE = 1 + GATHERED
HOT_P = 125
HOT_STEPS = HOT_ROWS // HOT_P
HALF_STEPS = HOT_STEPS // 2
LOOKUPS = 2 * HOT
TILE_COUNT = B // P
GROUP = 256
GROUPS = B // GROUP
TILES = GROUP // P
SLOTS = 2 * TILES
RAW_PLACES = TILES * N // HOT_STEPS
HALF = N // 2
UNITS = HALF + 1
CHUNKS = 3
UNIT_P = UNITS * N // CHUNKS
H1, H2 = 512, 256
H1_CHUNKS, H2_CHUNKS = H1 // P, H2 // P

BLOCK = 4
TILE_BLOCKS = P // BLOCK
GROUP_BLOCKS = GROUP // BLOCK
ROUND_BLOCKS = 16
TILE_ROUNDS = TILE_BLOCKS // ROUND_BLOCKS
ROUNDS = TILES * TILE_ROUNDS
PER_BANK = 4
TILE_BANKS = -(-HOT_FEATURE // PER_BANK)
TRANSPOSE_USES = TILES * TILE_BANKS
MLP_USES = H1_CHUNKS + H2_CHUNKS + 1

STEPS = [
    "B0 G0 H0 H1 Q0 G1 H2 Q1 H3 S0 Q2 H4 Q3 H5 W0 M0 H6 W1 M1 Q4 M2 H7 W2 M3".split(),
    "G0 H8 M4 H9 Q0 M5 H10 Q1 H11 M6 H12 Q2 H13 W3 Q3 H14 W4 Q4 H15 G1".split(),
]
LAST_STEPS = [
    "G0 Q0 G1 Q1 S0 Q2 M0 Q3 M1 Q4".split(),
    "G0 G1 M2 M3 M4 M5 M6".split(),
]
FIRST_STEPS = "H0 H1 H2 Q0 H3 H4 H5 Q1 H6 H7 H8 Q2 H9 H10 H11 Q3 H12 H13 Q4 H14 H15".split()


def dlrm_tower(nc, dense, ids, hot_ids, row_numbers, tables, w1_dense, w1_again, w1_units, b1, w2, b2, w3, identity, late_rows, bounce, y):
    ctx = ExitStack()
    with ctx:
        def sb(name, shape, dtype):
            return ctx.enter_context(nc.sbuf_tensor(name, shape, dtype))

        def ps(name, shape):
            return ctx.enter_context(nc.psum_tensor(name, shape, F32))

        def sem(name):
            return ctx.enter_context(nc.semaphore(name))

        identity_sb = sb("identity_sb", [P, P], F32)
        late_sb = sb("late_sb", [P, HALF], I32)
        w1d_sb = sb("w1d_sb", [P, H1], F32)
        w1u_hi = sb("w1u_hi", [UNIT_P, CHUNKS, H1], F32R)
        w1u_lo = sb("w1u_lo", [UNIT_P, CHUNKS, H1], F32R)
        w2_hi = sb("w2_hi", [P, H1_CHUNKS, H2], F32R)
        w2_lo = sb("w2_lo", [P, H1_CHUNKS, H2], F32R)
        w3_sb = sb("w3_sb", [P, H2_CHUNKS], F32)
        b1_sb = sb("b1_sb", [P, H1_CHUNKS], F32)
        b2_sb = sb("b2_sb", [P, H2_CHUNKS], F32)
        ids_sb = sb("ids_sb", [P, SLOTS, TABLES], I32)
        rows = sb("rows", [P, TILES, HOT_FEATURE, P], F32)
        hot_ids_sb = sb("hot_ids_sb", [P, B], F16)
        selector = sb("selector", [P, HOT], F16)
        row_numbers_sb = sb("row_numbers_sb", [HOT_P, HOT_STEPS], F32)
        table_hi = sb("table_hi", [HOT_P, HOT, HOT_STEPS, P], F32R)
        table_lo = sb("table_lo", [HOT_P, HOT, HOT_STEPS, P], F32R)
        one_hot = sb("one_hot", [HOT_P, 2, HALF_STEPS, GROUP], F32R)
        embed_t = sb("embed_t", [P, SLOTS, P, N], F32)
        units = sb("units", [P, 2, UNITS, GROUP_BLOCKS], F32)
        packed_hi = sb("packed_hi", [UNIT_P, BLOCK, CHUNKS, GROUP_BLOCKS], F32R)
        packed_lo = sb("packed_lo", [UNIT_P, BLOCK, CHUNKS, GROUP_BLOCKS], F32R)
        hidden1_hi = sb("hidden1_hi", [P, H1_CHUNKS, GROUP], F32R)
        hidden1_lo = sb("hidden1_lo", [P, H1_CHUNKS, GROUP], F32R)
        scratch = sb("scratch", [P, 4, GROUP], F32)
        y_sb = sb("y_sb", [P, TILE_COUNT], F32)

        def by_chunk(at):
            return at.rearrange("p (s c q) -> p s c q", s=BLOCK, c=CHUNKS)

        packed_raw = by_chunk(scratch[0:UNIT_P, 0:CHUNKS, :].rearrange("p c b -> p (c b)"))
        hidden1_raw = scratch[:, 0:2, :]
        last_packed_raw = by_chunk(rows[0:UNIT_P, 0, 0:2 * CHUNKS, :].rearrange("p c d -> p (c d)"))
        hidden2 = scratch[:, 2:4, :]
        y_rows = scratch[0:TILE_COUNT, 0, 0:P]

        place = embed_t[0:HOT_P, TILES:SLOTS].rearrange("p t b f -> p (t b f)")
        raw_tables = []
        for k in range(HOT):
            at = k % RAW_PLACES * HOT_STEPS * P
            raw_tables.append(place[:, at:at + HOT_STEPS * P].rearrange("p (j d) -> p j d", d=P))
        landing = [scratch[:, 0:2, :].rearrange("p c b -> p (c b)"), scratch[:, 2:4, :].rearrange("p c b -> p (c b)"),
                   units[:, 1].rearrange("p k q -> p (k q)")[:, 0:H1]]
        w1a_sb = landing[2]

        transpose_ps = ps("transpose_ps", [P, 2, PER_BANK, P])
        gram_ps = ps("gram_ps", [P, 2, 512])
        hot_ids_ps = ps("hot_ids_ps", [P, 512])
        hot_ps = ps("hot_ps", [P, 512])
        mlp_ps = ps("mlp_ps", [P, 2, 512])

        weights_loaded = sem("weights_loaded")
        pieces_loaded = sem("pieces_loaded")
        const_loaded = sem("const_loaded")
        late_loaded = sem("late_loaded")
        ids_loaded = [sem(f"ids_loaded{i}") for i in range(SLOTS)]
        gathered = [[sem(f"gathered{i}_{u}") for u in range(TILE_BANKS)] for i in range(TILES)]
        dense_loaded = [sem(f"dense_loaded{i}") for i in range(TILES)]
        raw_loaded = [sem(f"raw_loaded{k}") for k in range(HOT)]
        hi_split = sem("hi_split")
        lo_split = sem("lo_split")
        hot_ids_zeroed = sem("hot_ids_zeroed")
        hot_ids_loaded = sem("hot_ids_loaded")
        selector_ready = sem("selector_ready")
        hot_ids_ready = sem("hot_ids_ready")
        one_hot_ready = sem("one_hot_ready")
        hot_ready = sem("hot_ready")
        hot_copied = sem("hot_copied")
        banks_zeroed = sem("banks_zeroed")
        weights_hi = sem("weights_hi")
        weights_lo = sem("weights_lo")
        w1_summed = sem("w1_summed")
        gathers_begun = sem("gathers_begun")
        rounds_begun = sem("rounds_begun")
        transposed = sem("transposed")
        embed_copied = sem("embed_copied")
        gram_ready = sem("gram_ready")
        late_copied = sem("late_copied")
        early_copied = sem("early_copied")
        units_stored = sem("units_stored")
        units_packed = sem("units_packed")
        units_hi = sem("units_hi")
        units_lo = sem("units_lo")
        hidden1_split = sem("hidden1_split")
        mlp_ready = sem("mlp_ready")
        mlp_copied = sem("mlp_copied")
        y_stored = sem("y_stored")

        pieces = [(landing[c][0:UNIT_P], w1u_hi[:, c, :], w1u_lo[:, c, :]) for c in range(CHUNKS)]
        pieces.append((scratch[:, :, :], w2_hi[:, :, :], w2_lo[:, :, :]))

        def features(u):
            return range(PER_BANK * u, min(HOT_FEATURE, PER_BANK * (u + 1)))

        def gathers(u):
            return [f for f in features(u) if f > 0]

        def gram_slot(i, first, last):
            return gram_ps[:, i % 2, 0:ROUND_BLOCKS * N].rearrange("p (q m) -> p q m", m=N)[:, :, first:last]

        def unit_slot(buf, r, first, last):
            return units[:, buf, first:last, r * ROUND_BLOCKS:(r + 1) * ROUND_BLOCKS].rearrange("p k q -> p q k")

        block = ctx.enter_context(nc.Block())

        @block.sync
        def _(sp):
            def load_ids(t, slot):
                sp.dma_start(ids_sb[:, slot, :], ids[bass.ds(t * P, P), :]).then_inc(ids_loaded[slot], 16)

            def load_dense(t, t2):
                sp.dma_start(rows[:, t2, 0, :], dense[bass.ds(t * P, P), :]).then_inc(dense_loaded[t2], 16)

            def load_hot_table(k):
                if k >= RAW_PLACES:
                    sp.wait_ge(lo_split, k - RAW_PLACES + 1)
                sp.dma_start(raw_tables[k], tables[HOT_TABLES[k]].rearrange("(p j) d -> p j d", p=HOT_P)).then_inc(
                    raw_loaded[k], 16)

            def pack(g, buf, landing):
                sp.wait_ge(early_copied, ROUNDS * (g + 1))
                sp.dma_start(bounce, units[:, buf].rearrange("p k q -> p (k q)")).then_inc(units_stored, 16)
                sp.wait_ge(units_stored, 16 * (g + 1))
                by_row = bounce.rearrange("(s n) x -> s (n x)", s=BLOCK)[:, 0:N * UNITS * GROUP_BLOCKS]
                sp.dma_start(landing.rearrange("p s c q -> p s (c q)"),
                             by_row.rearrange("s (p x) -> p s x", p=UNIT_P)).then_inc(units_packed, 16)

            def group(g, buf, loads=(True, True), last_weights=False, landing=packed_raw):
                for t2 in range(TILES):
                    if loads[0]:
                        sp.wait_ge(transposed, TRANSPOSE_USES * g + TILE_BANKS * (t2 + 1))
                        load_dense(TILES * (g + 1) + t2, t2)
                    if loads[1]:
                        load_ids(TILES * (g + 2) + t2, buf * TILES + t2)
                if last_weights:
                    sp.wait_ge(weights_lo, CHUNKS)
                    sp.dma_start(scratch[:, :, :], w2.rearrange("(c p) h -> p c h", p=P)).then_inc(weights_loaded, 16)
                    sp.dma_start(w1a_sb, w1_again).then_inc(weights_loaded, 16)
                    sp.wait_ge(weights_lo, len(pieces))
                pack(g, buf, landing)

            load_ids(0, 0)
            sp.dma_start(identity_sb[:, :], identity).then_inc(const_loaded, 16)
            sp.dma_start(row_numbers_sb[:, :], row_numbers).then_inc(const_loaded, 16)
            load_hot_table(0)
            load_hot_table(1)
            for slot in range(1, SLOTS):
                load_ids(slot, slot)
            for t2 in range(TILES):
                load_dense(t2, t2)
            sp.dma_start(late_sb[:, :], late_rows).then_inc(late_loaded, 16)
            for k in range(2, min(HOT, RAW_PLACES)):
                load_hot_table(k)
            for c in range(CHUNKS):
                sp.dma_start(pieces[c][0], w1_units.rearrange("(p c) h -> c p h", c=CHUNKS)[c]).then_inc(pieces_loaded, 16)
            sp.dma_start(w1d_sb[:, :], w1_dense).then_inc(weights_loaded, 16)
            sp.dma_start(b1_sb[:, :], b1).then_inc(weights_loaded, 16)
            sp.dma_start(b2_sb[:, :], b2).then_inc(weights_loaded, 16)
            sp.dma_start(w3_sb[:, :], w3).then_inc(weights_loaded, 16)
            for k in range(RAW_PLACES, HOT):
                load_hot_table(k)
            group(0, 0, last_weights=True)
            group(1, 1)
            with sp.Fori(1, GROUPS // 2 - 1) as i:
                group(2 * i, 0)
                group(2 * i + 1, 1)
            group(GROUPS - 2, 0, loads=(True, False))
            sp.wait_ge(units_packed, 16 * (GROUPS - 1))
            group(GROUPS - 1, 1, loads=(False, False), landing=last_packed_raw)
            sp.wait_ge(mlp_copied, MLP_USES * GROUPS + 2)
            sp.dma_start(y.rearrange("(t p) c -> t (p c)", p=P), y_rows).then_inc(y_stored, 16)
            sp.wait_ge(y_stored, 16)

        @block.gpsimd
        def _(pool):
            def gather(i, slot, first):
                t2 = slot % TILES
                pool.wait_ge(ids_loaded[slot], 16 * (i + 1))
                if not first:
                    pool.sem_inc(gathers_begun, 1)
                for u in range(TILE_BANKS):
                    if not first:
                        pool.wait_ge(transposed, TILE_BANKS * (SLOTS * i + slot - TILES) + u + 1)
                        pool.sem_inc(gathers_begun, 1)
                    for f in gathers(u):
                        table = GATHERED_TABLES[f - 1]
                        nc.gpsimd.indirect_dma_start(
                            rows[:, t2, f, :], None, tables[table],
                            bass.IndirectOffsetOnAxis(ids_sb[:, slot, table:table + 1], 0)).then_inc(gathered[t2][u], 16)

            pool.wait_ge(hot_ids_zeroed, 1)
            nc.gpsimd.dma_start(hot_ids_sb[0:HOT, :], hot_ids).then_inc(hot_ids_loaded, 16)
            for slot in range(SLOTS):
                gather(0, slot, slot < TILES)
            with pool.Fori(1, TILE_COUNT // SLOTS) as i:
                for slot in range(SLOTS):
                    gather(i, slot, False)

        def next_tile(g, buf, t2):
            return (g, buf, 1) if t2 == 0 else (g + 1, 1 - buf, 0)

        @block.scalar
        def _(act):
            def embed_copy(g, buf, t2, u):
                use = t2 * TILE_BANKS + u
                act.wait_ge(transposed, TRANSPOSE_USES * g + use + 1)
                f = features(u)
                out = embed_t[:, buf * TILES + t2, :, f[0]:f[-1] + 1].rearrange("p b n -> p n b")
                nc.scalar.copy(out, transpose_ps[:, use % 2, 0:len(f), :]).then_inc(embed_copied, 1)

            def mlp_copy(g, buf, m):
                act.wait_ge(mlp_ready, MLP_USES * g + m + 1)
                src = mlp_ps[:, m % 2, 0:GROUP]
                if m < H1_CHUNKS:
                    if m >= 2:
                        act.wait_ge(hidden1_split, H1_CHUNKS * g + m - 1)
                    nc.scalar.activation(hidden1_raw[:, m % 2, :], src, ACT.Relu, bias=b1_sb[:, m:m + 1])
                    nc.scalar.activation(hidden1_hi[:, m, :], src, ACT.Relu, bias=b1_sb[:, m:m + 1]).then_inc(mlp_copied, 1)
                elif m < H1_CHUNKS + H2_CHUNKS:
                    c = m - H1_CHUNKS
                    nc.scalar.activation(hidden2[:, c, :].rearrange("p (q s) -> p s q", s=BLOCK),
                                         src.rearrange("p (s q) -> p s q", s=BLOCK),
                                         ACT.Relu, bias=b2_sb[:, c:c + 1]).then_inc(mlp_copied, 1)
                else:
                    nc.scalar.copy(y_sb[:, bass.ds(g * TILES, TILES)], src[:, 0:TILES]).then_inc(mlp_copied, 1)

            def units_upper(g, landing=packed_raw):
                act.wait_ge(units_packed, 16 * (g + 1))
                nc.scalar.copy(packed_hi[:, :, :, :], landing).then_inc(units_hi, 1)

            def late_columns(g, buf, r):
                act.wait_ge(gram_ready, ROUNDS * g + r + 1)
                nc.scalar.copy(unit_slot(buf, r, 0, UNITS), gram_slot(r, HALF, N)).then_inc(late_copied, 1)

            def hot_copy(g, k, buf):
                act.wait_ge(hot_ready, LOOKUPS * g + 2 * (k + 1))
                out = embed_t[:, buf * TILES:(buf + 1) * TILES, :, HOT_FEATURE + k]
                nc.scalar.copy(out, hot_ps[:, 0:GROUP].rearrange("p (t b) -> p t b", t=TILES)).then_inc(hot_copied, 1)

            def group(g, buf, steps, mlp_before=True):
                for t2 in range(TILES):
                    for step, n in [(x[0], int(x[1:])) for x in steps[t2]]:
                        if step == "G":
                            late_columns(g, buf, t2 * TILE_ROUNDS + n)
                        elif step == "Q":
                            embed_copy(*next_tile(g, buf, t2), n)
                        elif step == "H" and n % 2 == 1:
                            hot_copy(g + 1, n // 2, 1 - buf)
                        elif step == "S" and mlp_before:
                            units_upper(g - 1)
                        elif step == "M" and mlp_before:
                            mlp_copy(g - 1, 1 - buf, n)
                        elif step == "W" and not mlp_before and n < len(pieces):
                            weights_upper(n)

            act.sem_inc(mlp_copied, 1)

            def split_hi(k):
                act.wait_ge(raw_loaded[k], 16)
                nc.scalar.copy(table_hi[:, k], raw_tables[k]).then_inc(hi_split, 1)

            def weights_upper(n):
                if n < CHUNKS:
                    act.wait_ge(pieces_loaded, 16 * CHUNKS)
                else:
                    act.wait_ge(weights_loaded, 16 * 6)
                loaded, hi, _ = pieces[n]
                nc.scalar.copy(hi, loaded).then_inc(weights_hi, 1)

            split_hi(0)
            for step, n in [(x[0], int(x[1:])) for x in FIRST_STEPS]:
                if step == "H" and n % 2 == 0 and n // 2 + 1 < HOT:
                    split_hi(n // 2 + 1)
                elif step == "H" and n % 2 == 1:
                    hot_copy(0, n // 2, 0)
                elif step == "Q":
                    embed_copy(0, 0, 0, n)
            group(0, 0, STEPS, False)
            with act.Fori(0, GROUPS // 2 - 1) as i:
                group(2 * i + 1, 1, STEPS)
                group(2 * i + 2, 0, STEPS)
            group(GROUPS - 1, 1, LAST_STEPS)
            units_upper(GROUPS - 1, last_packed_raw)
            for m in range(MLP_USES):
                mlp_copy(GROUPS - 1, 1, m)
            act.wait_ge(mlp_ready, MLP_USES * GROUPS + 1)
            nc.scalar.copy(y_rows, mlp_ps[0:TILE_COUNT, 1, 0:P]).then_inc(mlp_copied, 1)

        @block.vector
        def _(dve):
            def early_columns(g, buf, r):
                dve.wait_ge(late_copied, ROUNDS * g + r + 1)
                dve.sem_inc(rounds_begun, 1)
                rows_taken = late_sb[:, None, :].to_broadcast([P, ROUND_BLOCKS, HALF])
                nc.vector.copy_predicated(unit_slot(buf, r, 1, UNITS), rows_taken, gram_slot(r, 0, HALF)).then_inc(
                    early_copied, 1)

            def make_one_hot(g, n, first=False):
                k, half = n // 2, n % 2
                if not first:
                    dve.wait_ge(hot_ready, LOOKUPS * g + n - 1)
                if half == 0:
                    dve.wait_ge(hot_ids_ready, HOT * g + k + 1)
                steps = slice(half * HALF_STEPS, (half + 1) * HALF_STEPS)
                ids_over = hot_ids_ps[0:HOT_P, None, 0:GROUP].to_broadcast([HOT_P, HALF_STEPS, GROUP])
                numbers_over = row_numbers_sb[:, steps, None].to_broadcast([HOT_P, HALF_STEPS, GROUP])
                nc.vector.tensor_tensor(one_hot[:, half], ids_over, numbers_over, ALU.is_equal).then_inc(one_hot_ready, 1)

            def lower(whole, hi, lo):
                return nc.vector.tensor_tensor(lo, whole, hi.bitcast(F32), ALU.subtract)

            def split_lo(k):
                dve.wait_ge(hi_split, k + 1)
                lower(raw_tables[k], table_hi[:, k], table_lo[:, k]).then_inc(lo_split, 1)

            def units_lower(g, landing=packed_raw):
                dve.wait_ge(units_hi, g + 1)
                lower(landing, packed_hi[:, :, :, :], packed_lo[:, :, :, :]).then_inc(units_lo, 1)

            def hidden1_lower(g, m):
                dve.wait_ge(mlp_copied, MLP_USES * g + m + 2)
                lower(hidden1_raw[:, m % 2, :], hidden1_hi[:, m, :], hidden1_lo[:, m, :]).then_inc(hidden1_split, 1)

            def group(g, buf, steps, mlp_before=True):
                for t2 in range(TILES):
                    for step, n in [(x[0], int(x[1:])) for x in steps[t2]]:
                        if step == "G":
                            early_columns(g, buf, t2 * TILE_ROUNDS + n)
                        elif step == "B":
                            make_one_hot(g + 1, 0)
                            make_one_hot(g + 1, 1)
                        elif step == "H" and n + 2 < LOOKUPS:
                            make_one_hot(g + 1, n + 2)
                        elif step == "S" and mlp_before:
                            units_lower(g - 1)
                        elif step == "M" and mlp_before and n < H1_CHUNKS:
                            hidden1_lower(g - 1, n)
                        elif step == "W" and not mlp_before and n < len(pieces):
                            dve.wait_ge(weights_hi, n + 1)
                            lower(*pieces[n]).then_inc(weights_lo, 1)
                        elif step == "W" and not mlp_before and n == len(pieces):
                            dve.wait_ge(weights_loaded, 16 * 6)
                            nc.vector.tensor_tensor(w1d_sb[:, :], w1d_sb[:, :], w1a_sb, ALU.add).then_inc(w1_summed, 1)

            nc.vector.memset(hot_ids_sb[:, :], 0.0).then_inc(hot_ids_zeroed, 1)
            nc.vector.memset(gram_ps[:, :, :], 0.0).then_inc(banks_zeroed, 1)
            dve.wait_ge(const_loaded, 16 * 2)
            nc.vector.tensor_copy(selector[:, :], identity_sb[:, 0:HOT]).then_inc(selector_ready, 1)
            make_one_hot(0, 0, first=True)
            split_lo(0)
            make_one_hot(0, 1, first=True)
            for step, n in [(x[0], int(x[1:])) for x in FIRST_STEPS]:
                if step == "H" and n % 2 == 0 and n // 2 + 1 < HOT:
                    split_lo(n // 2 + 1)
                if step == "H" and n + 2 < LOOKUPS:
                    make_one_hot(0, n + 2)
            dve.wait_ge(late_loaded, 16)
            group(0, 0, STEPS, False)
            with dve.Fori(0, GROUPS // 2 - 1) as i:
                group(2 * i + 1, 1, STEPS)
                group(2 * i + 2, 0, STEPS)
            group(GROUPS - 1, 1, LAST_STEPS)
            units_lower(GROUPS - 1, last_packed_raw)
            for m in range(H1_CHUNKS):
                hidden1_lower(GROUPS - 1, m)

        @block.tensor
        def _(pe):
            def transposes(g, buf, t2, u, first=False):
                use = t2 * TILE_BANKS + u
                if u == 0:
                    pe.wait_ge(dense_loaded[t2], 16 * (g + 1))
                pe.wait_ge(gathered[t2][u], 16 * len(gathers(u)) * (g + 1))
                if not (first and use < 2):
                    pe.wait_ge(embed_copied, TRANSPOSE_USES * g + use - 1)
                for i, f in enumerate(features(u)):
                    last = nc.tensor.transpose(transpose_ps[:, use % 2, i, :], rows[:, t2, f, :], identity_sb[:, :])
                last.then_inc(transposed, 1)

            def broadcast_ids(g, k):
                nc.tensor.matmul(hot_ids_ps[0:HOT_P, 0:GROUP], selector[:, k:k + 1].to_broadcast([P, HOT_P]),
                                 hot_ids_sb[:, bass.ds(g * GROUP, GROUP)],
                                 start=True, stop=True).then_inc(hot_ids_ready, 1)

            def look_up(g, n, first=False):
                k, half = n // 2, n % 2
                pe.wait_ge(one_hot_ready, LOOKUPS * g + n + 1)
                if half == 0 and first:
                    pe.wait_ge(lo_split, k + 1)
                if half == 0 and not (first and k == 0):
                    pe.wait_ge(hot_copied, HOT * g + k)
                for j in range(HALF_STEPS):
                    step = half * HALF_STEPS + j
                    for table in (table_hi, table_lo):
                        last = nc.tensor.matmul(hot_ps[:, 0:GROUP], table[:, k, step, :], one_hot[:, half, j, :],
                                                start=(step == 0 and table is table_hi),
                                                stop=(step == HOT_STEPS - 1 and table is table_lo))
                last.then_inc(hot_ready, 1)
                if half == 0 and k + 1 < HOT:
                    pe.wait_ge(one_hot_ready, LOOKUPS * g + n + 2)
                    broadcast_ids(g, k + 1)

            def gram(g, buf, t2, n, first):
                r = t2 * TILE_ROUNDS + n
                if n == 0:
                    done = (t2 + 1) * TILE_BANKS
                    pe.wait_ge(embed_copied, TRANSPOSE_USES * g + done)
                    pe.wait_ge(hot_copied, HOT * (g + 1))
                if not (first and r < 2):
                    pe.wait_ge(early_copied, ROUNDS * g + r - 1)
                slot = buf * TILES + t2
                for q in range(ROUND_BLOCKS):
                    for s in range(BLOCK):
                        b = (n * ROUND_BLOCKS + q) * BLOCK + s
                        last = nc.tensor.matmul(gram_ps[32 * s:32 * s + N, r % 2, q * N:(q + 1) * N],
                                                embed_t[:, slot, b, :], embed_t[:, slot, b, :], start=True, stop=True)
                last.then_inc(gram_ready, 1)

            def dense_columns(buf):
                whole = embed_t[:, buf * TILES:(buf + 1) * TILES, :, 0]
                return whole.rearrange("p t (q s) -> p s t q", s=BLOCK)

            def three_products(out, w, x, start, stop):
                nc.tensor.matmul(out, w[0], x[0], start=start, stop=False)
                nc.tensor.matmul(out, w[0], x[1], start=False, stop=False)
                return nc.tensor.matmul(out, w[1], x[0], start=False, stop=stop)

            def mlp(g, buf, m):
                out = mlp_ps[:, m % 2, 0:GROUP]
                need = H1_CHUNKS + H2_CHUNKS if m == H1_CHUNKS + H2_CHUNKS else max(m - 1, 0)
                pe.wait_ge(mlp_copied, MLP_USES * g + need + 1)
                if m < H1_CHUNKS:
                    h = slice(m * P, (m + 1) * P)
                    nc.tensor.matmul(out, w1d_sb[:, h], dense_columns(buf), start=True, stop=False)
                    if m == 0:
                        pe.wait_ge(units_lo, g + 1)
                    for c in range(CHUNKS):
                        last = three_products(out, (w1u_hi[:, c, h], w1u_lo[:, c, h]),
                                              (packed_hi[:, :, c, :], packed_lo[:, :, c, :]), False, c == CHUNKS - 1)
                elif m < H1_CHUNKS + H2_CHUNKS:
                    h = slice((m - H1_CHUNKS) * P, (m - H1_CHUNKS + 1) * P)
                    for c in range(H1_CHUNKS):
                        if m == H1_CHUNKS:
                            pe.wait_ge(hidden1_split, H1_CHUNKS * g + c + 1)
                        last = three_products(out, (w2_hi[:, c, h], w2_lo[:, c, h]),
                                              (hidden1_hi[:, c, :], hidden1_lo[:, c, :]), c == 0, c == H1_CHUNKS - 1)
                else:
                    for t in range(TILES):
                        for c in range(H2_CHUNKS):
                            last = nc.tensor.matmul(out[:, t:t + 1], hidden2[:, c, t * P:(t + 1) * P], w3_sb[:, c:c + 1],
                                                    start=(c == 0), stop=(c == H2_CHUNKS - 1))
                last.then_inc(mlp_ready, 1)

            def group(g, buf, steps, first=False):
                for t2 in range(TILES):
                    for step, n in [(x[0], int(x[1:])) for x in steps[t2]]:
                        if step == "G":
                            gram(g, buf, t2, n, first)
                        elif step == "Q":
                            transposes(*next_tile(g, buf, t2), n)
                        elif step == "B":
                            broadcast_ids(g + 1, 0)
                        elif step == "H":
                            look_up(g + 1, n)
                        elif step == "M" and not first:
                            mlp(g - 1, 1 - buf, n)

            pe.wait_ge(const_loaded, 16 * 2)
            pe.wait_ge(selector_ready, 1)
            pe.wait_ge(hot_ids_loaded, 16)
            broadcast_ids(0, 0)
            for step, n in [(x[0], int(x[1:])) for x in FIRST_STEPS]:
                if step == "H":
                    look_up(0, n, first=True)
                else:
                    transposes(0, 0, 0, n, first=True)
            pe.wait_ge(banks_zeroed, 1)
            group(0, 0, STEPS, first=True)
            pe.wait_ge(w1_summed, 1)
            pe.wait_ge(weights_loaded, 16 * 6)
            pe.wait_ge(weights_lo, len(pieces))
            with pe.Fori(0, GROUPS // 2 - 1) as i:
                group(2 * i + 1, 1, STEPS)
                group(2 * i + 2, 0, STEPS)
            group(GROUPS - 1, 1, LAST_STEPS)
            for m in range(MLP_USES):
                mlp(GROUPS - 1, 1, m)
            pe.wait_ge(mlp_copied, MLP_USES * GROUPS + 1)
            nc.tensor.transpose(mlp_ps[0:TILE_COUNT, 1, 0:P], y_sb[:, :], identity_sb[:, :]).then_inc(mlp_ready, 1)


def unit_rows():
    def pair(i, j):
        i, j = min(i, j), max(i, j)
        return P + i * N - i * (i + 1) // 2 + (j - i - 1)

    seen, rows = set(), -np.ones((N, UNITS), int)
    for k in range(UNITS):
        for n in range(N):
            m = k - 1 if k and k <= n < k + HALF else HALF + k
            row = pair(FEATURES[n], FEATURES[m]) if n != m else -1
            if row not in seen | {-1}:
                seen.add(row)
                rows[n, k] = row
    assert len(seen) == N * (N - 1) // 2
    return rows.reshape(-1)


def by_partition(x):
    return np.ascontiguousarray(x.reshape(-1, P).T)


def kernel(**inputs):
    import concourse.bacc as bacc
    from concourse.bass_utils import run_bass_kernel_spmd

    a = {name: np.asarray(x) for name, x in inputs.items()}
    pairs = P + N * (N - 1) // 2
    w1 = a["W_top1"]
    where = unit_rows()
    w1_units = np.zeros((UNITS * N, H1), w1.dtype)
    w1_units[where >= 0] = w1[where[where >= 0]]
    late = np.zeros((BLOCK, 32, HALF), np.int32)
    for k in range(1, UNITS):
        late[:, k:k + HALF, k - 1] = 1
    given = {
        "dense": a["r_dense_features"], "ids": a["ids"], "hot_ids": np.ascontiguousarray(a["ids"].T[HOT_TABLES]),
        "row_numbers": np.arange(HOT_ROWS, dtype=np.float32).reshape(HOT_P, HOT_STEPS),
        **{f"table{f}": a[f"tbl_{f}"] for f in range(TABLES)},
        "w1_dense": np.ascontiguousarray(w1[0:P]), "w1_again": np.ascontiguousarray(w1[pairs:]), "w1_units": w1_units,
        "b1": by_partition(a["b_top1"]), "w2": a["W_top2"], "b2": by_partition(a["b_top2"]), "w3": by_partition(a["W_top3"]),
        "identity": np.eye(P, dtype=np.float32), "late_rows": late.reshape(P, HALF),
    }
    nc = bacc.Bacc("TRN2", target_bir_lowering=False, num_devices=1)
    aps = {n: nc.dram_tensor(n, x.shape, mybir.dt.from_np(x.dtype), kind="ExternalInput").ap() for n, x in given.items()}
    y = nc.dram_tensor("y", (B, 1), F32, kind="ExternalOutput").ap()
    bounce = nc.dram_tensor("bounce", (P, UNITS * GROUP_BLOCKS), F32, kind="Internal").ap()
    tables = [aps.pop(f"table{f}") for f in range(TABLES)]
    dlrm_tower(nc, tables=tables, bounce=bounce, y=y, **aps)
    result = run_bass_kernel_spmd(nc, [given], core_ids=[0])
    return result.results[0]["y"]
```
